# Optimizing a Trainium2 kernel written in Bass

```python
import numpy as np
import jax
import jax.numpy as jnp

def _softmax(x, axis=-1):
    return jax.nn.softmax(x, axis=axis)

def _gelu(x):
    return jax.nn.gelu(x, approximate=True)

def _silu(x):
    return jax.nn.silu(x)

def _sigmoid(x):
    return jax.nn.sigmoid(x)

def _layernorm(x, axis=-1, eps=1e-05):
    m = jnp.mean(x, axis=axis, keepdims=True)
    v = jnp.var(x, axis=axis, keepdims=True)
    return (x - m) / jnp.sqrt(v + eps)

def _scatter_add(tgt, idx, src, axis=0):
    return tgt.at[idx].add(src)

def _segment_sum(src, seg, n):
    return jax.ops.segment_sum(src, seg, n)
kernel_name = 'mk_dlrm_tower_d1_rec_r8_5defe3'

def setup_inputs(seed: int=0):
    np.random.seed(seed)
    _w = jnp.asarray

    def _rec_inputs():
        import jax
        import jax.numpy as jnp
        _tk = jax.random.key(seed)
        ids = jnp.stack([jax.random.randint(jax.random.fold_in(_tk, 200 + f), (512,), 0, v, jnp.int32) for f, v in enumerate([125000, 12500, 1000, 12500, 12500, 1000, 12500, 12500, 1250, 1000, 12500, 1000, 1250, 1000, 1250, 12500, 1250, 12500, 1000, 1250, 1000, 1250, 1000, 1000, 1250, 1250])], axis=1)
        tbl_0 = 0.05 * jax.random.normal(jax.random.fold_in(_tk, 500 + 0), (125000, 128), jnp.float32)
        tbl_1 = 0.05 * jax.random.normal(jax.random.fold_in(_tk, 500 + 1), (12500, 128), jnp.float32)
        tbl_2 = 0.05 * jax.random.normal(jax.random.fold_in(_tk, 500 + 2), (1000, 128), jnp.float32)
        tbl_3 = 0.05 * jax.random.normal(jax.random.fold_in(_tk, 500 + 3), (12500, 128), jnp.float32)
        tbl_4 = 0.05 * jax.random.normal(jax.random.fold_in(_tk, 500 + 4), (12500, 128), jnp.float32)
        tbl_5 = 0.05 * jax.random.normal(jax.random.fold_in(_tk, 500 + 5), (1000, 128), jnp.float32)
        tbl_6 = 0.05 * jax.random.normal(jax.random.fold_in(_tk, 500 + 6), (12500, 128), jnp.float32)
        tbl_7 = 0.05 * jax.random.normal(jax.random.fold_in(_tk, 500 + 7), (12500, 128), jnp.float32)
        tbl_8 = 0.05 * jax.random.normal(jax.random.fold_in(_tk, 500 + 8), (1250, 128), jnp.float32)
        tbl_9 = 0.05 * jax.random.normal(jax.random.fold_in(_tk, 500 + 9), (1000, 128), jnp.float32)
        tbl_10 = 0.05 * jax.random.normal(jax.random.fold_in(_tk, 500 + 10), (12500, 128), jnp.float32)
        tbl_11 = 0.05 * jax.random.normal(jax.random.fold_in(_tk, 500 + 11), (1000, 128), jnp.float32)
        tbl_12 = 0.05 * jax.random.normal(jax.random.fold_in(_tk, 500 + 12), (1250, 128), jnp.float32)
        tbl_13 = 0.05 * jax.random.normal(jax.random.fold_in(_tk, 500 + 13), (1000, 128), jnp.float32)
        tbl_14 = 0.05 * jax.random.normal(jax.random.fold_in(_tk, 500 + 14), (1250, 128), jnp.float32)
        tbl_15 = 0.05 * jax.random.normal(jax.random.fold_in(_tk, 500 + 15), (12500, 128), jnp.float32)
        tbl_16 = 0.05 * jax.random.normal(jax.random.fold_in(_tk, 500 + 16), (1250, 128), jnp.float32)
        tbl_17 = 0.05 * jax.random.normal(jax.random.fold_in(_tk, 500 + 17), (12500, 128), jnp.float32)
        tbl_18 = 0.05 * jax.random.normal(jax.random.fold_in(_tk, 500 + 18), (1000, 128), jnp.float32)
        tbl_19 = 0.05 * jax.random.normal(jax.random.fold_in(_tk, 500 + 19), (1250, 128), jnp.float32)
        tbl_20 = 0.05 * jax.random.normal(jax.random.fold_in(_tk, 500 + 20), (1000, 128), jnp.float32)
        tbl_21 = 0.05 * jax.random.normal(jax.random.fold_in(_tk, 500 + 21), (1250, 128), jnp.float32)
        tbl_22 = 0.05 * jax.random.normal(jax.random.fold_in(_tk, 500 + 22), (1000, 128), jnp.float32)
        tbl_23 = 0.05 * jax.random.normal(jax.random.fold_in(_tk, 500 + 23), (1000, 128), jnp.float32)
        tbl_24 = 0.05 * jax.random.normal(jax.random.fold_in(_tk, 500 + 24), (1250, 128), jnp.float32)
        tbl_25 = 0.05 * jax.random.normal(jax.random.fold_in(_tk, 500 + 25), (1250, 128), jnp.float32)
        _rk = jax.random.fold_in(_tk, 7)
        r_bottom_output = -0.000520686 + 1.00062 * jax.random.normal(jax.random.fold_in(_rk, 101), (512, 128), jnp.float32)
        W_top1 = 0.0456912 * jax.random.normal(jax.random.fold_in(_tk, 801), (479, 512), jnp.float32)
        W_top2 = 0.0441942 * jax.random.normal(jax.random.fold_in(_tk, 802), (512, 256), jnp.float32)
        W_top3 = 0.0625 * jax.random.normal(jax.random.fold_in(_tk, 803), (256, 1), jnp.float32)
        b_top1 = jnp.zeros((512,), jnp.float32)
        b_top2 = jnp.zeros((256,), jnp.float32)
        return (r_bottom_output, ids, tbl_0, tbl_1, tbl_2, tbl_3, tbl_4, tbl_5, tbl_6, tbl_7, tbl_8, tbl_9, tbl_10, tbl_11, tbl_12, tbl_13, tbl_14, tbl_15, tbl_16, tbl_17, tbl_18, tbl_19, tbl_20, tbl_21, tbl_22, tbl_23, tbl_24, tbl_25, W_top1, b_top1, W_top2, b_top2, W_top3)
    r_bottom_output, ids, tbl_0, tbl_1, tbl_2, tbl_3, tbl_4, tbl_5, tbl_6, tbl_7, tbl_8, tbl_9, tbl_10, tbl_11, tbl_12, tbl_13, tbl_14, tbl_15, tbl_16, tbl_17, tbl_18, tbl_19, tbl_20, tbl_21, tbl_22, tbl_23, tbl_24, tbl_25, W_top1, b_top1, W_top2, b_top2, W_top3 = _rec_inputs()

    def _L0_rec_setup():
        import jax, jax.numpy as jnp
        import numpy as np
        NUM_FEATURES = 27
        _TRIU_I, _TRIU_J = np.triu_indices(NUM_FEATURES, k=1)
        key = jax.random.key(seed)
        k1, k2 = jax.random.split(key)
        bottom_output = jax.random.normal(k1, (2048, 128), dtype=jnp.float32)
        embeddings = jax.random.normal(k2, (2048, 26, 128), dtype=jnp.float32)
        return {'bottom_output': bottom_output, 'embeddings': embeddings}
    _L0_rec_all = _L0_rec_setup()
    _L0_rec_in = {k: v for k, v in _L0_rec_all.items() if k in ()}
    del _L0_rec_all
    return {'r_bottom_output': r_bottom_output, 'ids': ids, 'tbl_0': tbl_0, 'tbl_1': tbl_1, 'tbl_2': tbl_2, 'tbl_3': tbl_3, 'tbl_4': tbl_4, 'tbl_5': tbl_5, 'tbl_6': tbl_6, 'tbl_7': tbl_7, 'tbl_8': tbl_8, 'tbl_9': tbl_9, 'tbl_10': tbl_10, 'tbl_11': tbl_11, 'tbl_12': tbl_12, 'tbl_13': tbl_13, 'tbl_14': tbl_14, 'tbl_15': tbl_15, 'tbl_16': tbl_16, 'tbl_17': tbl_17, 'tbl_18': tbl_18, 'tbl_19': tbl_19, 'tbl_20': tbl_20, 'tbl_21': tbl_21, 'tbl_22': tbl_22, 'tbl_23': tbl_23, 'tbl_24': tbl_24, 'tbl_25': tbl_25, 'W_top1': W_top1, 'b_top1': b_top1, 'W_top2': W_top2, 'b_top2': b_top2, 'W_top3': W_top3}

def reference(r_bottom_output, ids, tbl_0, tbl_1, tbl_2, tbl_3, tbl_4, tbl_5, tbl_6, tbl_7, tbl_8, tbl_9, tbl_10, tbl_11, tbl_12, tbl_13, tbl_14, tbl_15, tbl_16, tbl_17, tbl_18, tbl_19, tbl_20, tbl_21, tbl_22, tbl_23, tbl_24, tbl_25, W_top1, b_top1, W_top2, b_top2, W_top3):
    import jax
    import jax.numpy as jnp

    def _L0_rec_ref(bottom_output, embeddings):
        import jax, jax.numpy as jnp
        import numpy as np
        NUM_FEATURES = 27
        _TRIU_I, _TRIU_J = np.triu_indices(NUM_FEATURES, k=1)
        all_emb = jnp.concatenate([bottom_output[:, None, :], embeddings], axis=1)
        gram = jnp.einsum('bfd,bgd->bfg', all_emb, all_emb)
        return gram[:, _TRIU_I, _TRIU_J]
    e = jnp.stack([tbl_0[ids[:, 0]], tbl_1[ids[:, 1]], tbl_2[ids[:, 2]], tbl_3[ids[:, 3]], tbl_4[ids[:, 4]], tbl_5[ids[:, 5]], tbl_6[ids[:, 6]], tbl_7[ids[:, 7]], tbl_8[ids[:, 8]], tbl_9[ids[:, 9]], tbl_10[ids[:, 10]], tbl_11[ids[:, 11]], tbl_12[ids[:, 12]], tbl_13[ids[:, 13]], tbl_14[ids[:, 14]], tbl_15[ids[:, 15]], tbl_16[ids[:, 16]], tbl_17[ids[:, 17]], tbl_18[ids[:, 18]], tbl_19[ids[:, 19]], tbl_20[ids[:, 20]], tbl_21[ids[:, 21]], tbl_22[ids[:, 22]], tbl_23[ids[:, 23]], tbl_24[ids[:, 24]], tbl_25[ids[:, 25]]], axis=1)
    z = _L0_rec_ref(r_bottom_output, e)
    z = z.reshape(z.shape[0], -1)
    h = jnp.concatenate([z, r_bottom_output], axis=1)
    h = jnp.maximum(h @ W_top1 + b_top1, 0.0)
    h = jnp.maximum(h @ W_top2 + b_top2, 0.0)
    y = h @ W_top3
    return y

_drawn_inputs = setup_inputs


def setup_inputs(seed=0):
    import zlib

    import numpy as np

    out = dict(_drawn_inputs(seed))
    spreads = {'b_top1': (0.0, 0.1), 'b_top2': (0.0, 0.1)}
    factors = {}
    for name, (base, spread) in spreads.items():
        noise = np.random.default_rng([zlib.crc32(name.encode()), seed]).standard_normal(out[name].shape)
        drawn = base * np.exp(spread * noise) if base else spread * noise
        out[name] = jnp.asarray(drawn.astype(out[name].dtype))
    for name, factor in factors.items():
        out[name] = (out[name] * factor).astype(out[name].dtype)
    return out
```

```python
from contextlib import ExitStack

import concourse.bass as bass
from concourse import mybir

FP32 = mybir.dt.float32
ALU = mybir.AluOpType
ACT = mybir.ActivationFunctionType


def dlrm_program(nc, bottom, ids, tables, W1, b1, W2, b2, W3, y_out):
    P = 128
    B, D = bottom.shape
    TABLES = len(tables)
    F = TABLES + 1
    TILES = B // P
    FS = 32
    GS = P // FS
    GROUPS = P // GS
    H1, H2 = W2.shape
    N1, N2 = H1 // P, H2 // P

    TU = 4
    xunits = [list(range(f, min(f + TU, F))) for f in range(0, F, TU)]
    NX = len(xunits)
    XA = [u for u in range(NX) if u % 2 == 0]
    XV = [u for u in range(NX) if u % 2 == 1]

    GB = 4
    GU = 2 * GB
    NG = GROUPS // GU

    CH = 3
    rows = [F - 1 - CH * m for m in range(F // CH)]
    first_row = [sum(rows[:m]) for m in range(len(rows))]
    KZ = sum(rows)

    ctx = ExitStack()
    with ctx:
        def sb(name, shape, dt=FP32):
            return ctx.enter_context(nc.sbuf_tensor(name, shape, dt))

        def pb(name, shape):
            return ctx.enter_context(nc.psum_tensor(name, shape, FP32))

        def sem(name):
            return ctx.enter_context(nc.semaphore(name))

        idx = sb("idx", [P, TILES, TABLES], mybir.dt.int32)
        feat = sb("feat", [P, TILES, F, D])
        featT = sb("featT", [D, B, FS])
        bottomT = sb("bottomT", [D, B])
        ident = sb("ident", [P, P])
        z = sb("z", [F, 2, F, P])
        zT = sb("zT", [P, 2, CH, P])
        w1z = sb("w1z", [P, CH, H1])
        w1b = sb("w1b", [D, H1])
        w2 = sb("w2", [P, N1, H2])
        w3 = sb("w3", [P, N2])
        b1c = sb("b1c", [P, N1])
        b2c = sb("b2c", [P, N2])
        h1 = sb("h1", [P, N1, P])
        h2 = sb("h2", [P, N2, P])
        y = sb("y", [1, B])

        psX = [pb(f"psX{i}", [P, TU, P]) for i in range(2)]
        psG = [pb(f"psG{i}", [P, 2, 512]) for i in range(2)]
        psL = [pb(f"psL{i}", [P, 4, P]) for i in range(2)]

        idx_in = sem("idx_in")
        bottom_in = sem("bottom_in")
        rows_in = [[sem(f"rows_in_{t}_{u}") for u in range(NX)] for t in range(TILES)]
        w1_zeroed = sem("w1_zeroed")
        weights_in = sem("weights_in")
        ident_zeroed = sem("ident_zeroed")
        ident_made = sem("ident_made")
        pads_zeroed = sem("pads_zeroed")
        xposed = sem("xposed")
        xcopied_a = sem("xcopied_a")
        xcopied_v = sem("xcopied_v")
        gram_done = sem("gram_done")
        zcopied_a = sem("zcopied_a")
        zcopied_v = sem("zcopied_v")
        packed = [sem(f"packed_{i}") for i in range(2)]
        l1_done = sem("l1_done")
        h1_a = sem("h1_a")
        h1_v = sem("h1_v")
        l2_done = sem("l2_done")
        h2_a = sem("h2_a")
        h2_v = sem("h2_v")
        l3_done = sem("l3_done")
        y_made = sem("y_made")
        y_out_done = sem("y_out_done")

        block = ctx.enter_context(nc.Block())

        PACKS = len(rows)

        def gram_block(n, s):
            v = psG[n % 2][FS * s:FS * s + F, :, 0:GB * GS * F]
            return v.rearrange("i k (g s j) -> i s j k g", g=GB, s=GS)[:, s]

        def z_block(t, n, s):
            b0 = GS * GU * (n % NG)
            v = z[:, t % 2, :, b0:b0 + GS * GU].rearrange("i j (k g s) -> i s j k g", k=2, s=GS)
            return v[:, s]

        @block.sync
        def _(sp):
            sp.dma_start(idx[:], ids.rearrange("(t p) f -> p t f", p=P)).then_inc(idx_in, 16)
            sp.dma_start(feat[:, :, 0, :], bottom.rearrange("(t p) d -> p t d", p=P)).then_inc(bottom_in, 16)
            sp.dma_start(w1b[:], W1[W1.shape[0] - D:, :]).then_inc(weights_in, 16)
            sp.dma_start(w2[:], W2.rearrange("(k p) n -> p k n", p=P)).then_inc(weights_in, 16)
            with nc.allow_non_contiguous_dma(reason="a bias or a weight column over partitions"):
                sp.dma_start(w3[:], W3.rearrange("(k p) o -> p (k o)", p=P)).then_inc(weights_in, 16)
                sp.dma_start(b1c[:], b1.rearrange("(k p) -> p k", p=P)).then_inc(weights_in, 16)
                sp.dma_start(b2c[:], b2.rearrange("(k p) -> p k", p=P)).then_inc(weights_in, 16)
            sp.wait_ge(w1_zeroed, 1)
            start = 0
            for i in range(F - 1):
                n = F - 1 - i
                p0 = first_row[i // CH] + rows[i // CH] - n
                sp.dma_start(w1z[p0:p0 + n, i % CH, :], W1[start:start + n, :]).then_inc(weights_in, 16)
                start += n
            for t in range(TILES):
                sp.wait_ge(zcopied_a, 2 * NG * (t + 1))
                sp.wait_ge(zcopied_v, 2 * NG * (t + 1))
                if t >= 2:
                    sp.wait_ge(l1_done, t - 1)
                for m in range(PACKS):
                    sp.dma_start(zT[first_row[m]:first_row[m] + rows[m], t % 2, :, :],
                                 z[CH * m + 1:F, t % 2, CH * m:CH * m + CH, :]).then_inc(packed[t % 2], 16)
            sp.wait_ge(y_made, TILES)
            sp.dma_start(y_out.rearrange("b o -> o b"), y[0:1, :]).then_inc(y_out_done, 16)
            sp.wait_ge(y_out_done, 16)

        @block.gpsimd
        def _(pool):
            nc.gpsimd.memset(ident[:], 0.0).then_inc(ident_zeroed, 1)
            pool.wait_ge(ident_zeroed, 1)
            nc.gpsimd.affine_select(out=ident[:], in_=ident[:], compare_op=ALU.not_equal, fill=1.0, base=0,
                                    pattern=[[-1, P]], channel_multiplier=1).then_inc(ident_made, 1)
            pool.wait_ge(idx_in, 16)
            for t in range(TILES):
                for u, unit in enumerate(xunits):
                    for f in unit:
                        if f:
                            nc.gpsimd.indirect_dma_start(
                                feat[:, t, f, :], None, tables[f - 1],
                                bass.IndirectOffsetOnAxis(idx[:, t, f - 1:f], 0)).then_inc(rows_in[t][u], 16)

        @block.tensor
        def _(pe):
            pe.wait_ge(ident_made, 1)
            pe.wait_ge(bottom_in, 16)
            for t in range(TILES):
                for u, unit in enumerate(xunits):
                    n = NX * t + u
                    pe.wait_ge(rows_in[t][u], 16 * sum(f > 0 for f in unit))
                    if n >= 2:
                        before = (n - 2) % NX
                        done, mine = (xcopied_a, XA) if before in XA else (xcopied_v, XV)
                        pe.wait_ge(done, len(mine) * ((n - 2) // NX) + mine.index(before) + 1)
                    for k, f in enumerate(unit):
                        last = nc.tensor.transpose(psX[n % 2][:, k, :], feat[:, t, f, :], ident[:])
                    last.then_inc(xposed, 1)
                pe.wait_ge(xcopied_a, len(XA) * (t + 1))
                pe.wait_ge(xcopied_v, len(XV) * (t + 1))
                if t == 0:
                    pe.wait_ge(pads_zeroed, 1)
                for v in range(NG):
                    n = NG * t + v
                    if n >= 2:
                        pe.wait_ge(zcopied_a, 2 * (n - 1))
                        pe.wait_ge(zcopied_v, 2 * (n - 1))
                    for g in range(GU):
                        out = psG[n % 2][:, g // GB, (g % GB) * GS * F:(g % GB + 1) * GS * F]
                        b0 = P * t + GS * (GU * v + g)
                        last = nc.tensor.matmul(out, featT[:, b0:b0 + GS, :].rearrange("d s f -> d (s f)"),
                                                featT[:, b0:b0 + GS, 0:F], start=True, stop=True)
                    last.then_inc(gram_done, 1)
                if t == 0:
                    pe.wait_ge(weights_in, 16 * (5 + F - 1))
                if t >= 1:
                    pe.wait_ge(h2_a, t)
                    pe.wait_ge(y_made, t)
                pe.wait_ge(packed[t % 2], 16 * PACKS * (t // 2 + 1))
                for o in range(N1):
                    for c in range(CH):
                        nc.tensor.matmul(psL[o // 2][:, o % 2, :], w1z[0:KZ, c, P * o:P * (o + 1)], zT[0:KZ, t % 2, c, :],
                                         start=(c == 0), stop=False)
                    last = nc.tensor.matmul(psL[o // 2][:, o % 2, :], w1b[:, P * o:P * (o + 1)],
                                            bottomT[:, P * t:P * (t + 1)], start=False, stop=True)
                last.then_inc(l1_done, 1)
                pe.wait_ge(h1_a, 2 * (t + 1))
                pe.wait_ge(h1_v, 2 * (t + 1))
                for o in range(N2):
                    for c in range(N1):
                        last = nc.tensor.matmul(psL[o][:, 2, :], w2[:, c, P * o:P * (o + 1)],
                                                h1[:, c, :], start=(c == 0), stop=(c == N1 - 1))
                last.then_inc(l2_done, 1)
                pe.wait_ge(h2_a, t + 1)
                pe.wait_ge(h2_v, t + 1)
                for c in range(N2):
                    last = nc.tensor.matmul(psL[1][0:1, 3, :], w3[:, c:c + 1], h2[:, c, :],
                                            start=(c == 0), stop=(c == N2 - 1))
                last.then_inc(l3_done, 1)

        def featT_slots(t, unit):
            return featT[:, P * t:P * (t + 1), unit[0]:unit[-1] + 1]

        @block.scalar
        def _(act):
            for t in range(TILES):
                for u in XA:
                    n = NX * t + u
                    act.wait_ge(xposed, n + 1)
                    k = len(xunits[u])
                    if u == 0:
                        nc.scalar.activation(bottomT[:, P * t:P * (t + 1)], psX[n % 2][:, 0, :], ACT.Copy)
                    nc.scalar.activation(featT_slots(t, xunits[u]),
                                         psX[n % 2][:, 0:k, :].rearrange("d f b -> d b f"),
                                         ACT.Copy).then_inc(xcopied_a, 1)
                for v in range(NG):
                    n = NG * t + v
                    act.wait_ge(gram_done, n + 1)
                    if v == 0 and t >= 2:
                        act.wait_ge(packed[t % 2], 16 * PACKS * (t // 2))
                    for s in (0, 1):
                        nc.scalar.activation(z_block(t, n, s), gram_block(n, s), ACT.Copy).then_inc(zcopied_a, 1)
                act.wait_ge(l1_done, t + 1)
                if t == 0:
                    act.wait_ge(weights_in, 16 * (5 + F - 1))
                for o in (0, 1):
                    nc.scalar.activation(h1[:, o, :], psL[o // 2][:, o % 2, :], ACT.Relu, bias=b1c[:, o:o + 1]).then_inc(h1_a, 1)
                act.wait_ge(l2_done, t + 1)
                nc.scalar.activation(h2[:, 0, :], psL[0][:, 2, :], ACT.Relu, bias=b2c[:, 0:1]).then_inc(h2_a, 1)

        @block.vector
        def _(dve):
            nc.vector.memset(w1z[:], 0.0).then_inc(w1_zeroed, 1)
            nc.vector.memset(featT[:, :, F:FS], 0.0).then_inc(pads_zeroed, 1)
            for t in range(TILES):
                for u in XV:
                    n = NX * t + u
                    dve.wait_ge(xposed, n + 1)
                    k = len(xunits[u])
                    nc.vector.tensor_copy(featT_slots(t, xunits[u]),
                                          psX[n % 2][:, 0:k, :].rearrange("d f b -> d b f")).then_inc(xcopied_v, 1)
                for v in range(NG):
                    n = NG * t + v
                    dve.wait_ge(gram_done, n + 1)
                    if v == 0 and t >= 2:
                        dve.wait_ge(packed[t % 2], 16 * PACKS * (t // 2))
                    for s in (2, 3):
                        nc.vector.tensor_copy(z_block(t, n, s), gram_block(n, s)).then_inc(zcopied_v, 1)
                dve.wait_ge(l1_done, t + 1)
                if t == 0:
                    dve.wait_ge(weights_in, 16 * (5 + F - 1))
                for o in (2, 3):
                    nc.vector.tensor_scalar(h1[:, o, :], psL[o // 2][:, o % 2, :], b1c[:, o:o + 1], 0.0,
                                            ALU.add, ALU.max).then_inc(h1_v, 1)
                dve.wait_ge(l2_done, t + 1)
                nc.vector.tensor_scalar(h2[:, 1, :], psL[1][:, 2, :], b2c[:, 1:2], 0.0,
                                        ALU.add, ALU.max).then_inc(h2_v, 1)
                dve.wait_ge(l3_done, t + 1)
                nc.vector.tensor_copy(y[0:1, P * t:P * (t + 1)], psL[1][0:1, 3, :]).then_inc(y_made, 1)


def kernel(**inputs):
    import numpy as _np
    import concourse.bacc as _bacc
    from concourse import mybir as _mybir
    from concourse.bass_utils import run_bass_kernel_spmd as _run

    nc = _bacc.Bacc("TRN2", target_bir_lowering=False, num_devices=1)
    table_names = [f"tbl_{i}" for i in range(26)]
    arrays, args = {}, {}
    for name in ["r_bottom_output", "ids", *table_names, "W_top1", "b_top1", "W_top2", "b_top2", "W_top3"]:
        a = _np.ascontiguousarray(inputs[name])
        arrays[f"in_{name}"] = a
        args[name] = nc.dram_tensor(f"in_{name}", a.shape, _mybir.dt.from_np(a.dtype), kind="ExternalInput").ap()
    y = nc.dram_tensor("out_y", (inputs["ids"].shape[0], 1), _mybir.dt.float32, kind="ExternalOutput").ap()
    dlrm_program(nc, args["r_bottom_output"], args["ids"], [args[n] for n in table_names], args["W_top1"],
                 args["b_top1"], args["W_top2"], args["b_top2"], args["W_top3"], y)
    r = _run(nc, [arrays], core_ids=[0])
    return r.results[0]["out_y"]
```

```python
from contextlib import ExitStack

import concourse.bass as bass
from concourse import mybir

FP32 = mybir.dt.float32
FP32R = mybir.dt.float32r
INT32 = mybir.dt.int32
ALU = mybir.AluOpType
ACT = mybir.ActivationFunctionType


def feature_slots(small, F):
    return [0] + [f for f in range(1, F) if f not in small] + small


def triangle(F, CH):
    rows = [F - 1 - CH * m for m in range(F // CH)]
    return rows, [sum(rows[:m]) for m in range(len(rows))]


def dlrm_program(nc, bottom_t, ids, ids_t, tables, small, w1_pairs, w1_bottom, b1, W2, b2, W3, y_out):
    P = 128
    D, B = bottom_t.shape
    TABLES = len(tables)
    F = TABLES + 1
    TILES = B // P
    FS = 32
    GS = P // FS
    GROUPS = P // GS
    H1, H2 = W2.shape
    N1, N2 = H1 // P, H2 // P

    NR = 8
    Q = tables[small[0] - 1].shape[0] // NR
    assert all(tables[f - 1].shape[0] == NR * Q for f in small)
    L = len(small)

    def by_act(q):
        return 1 if q < L else 2

    def chunks_a(q):
        return sum(by_act(i) for i in range(q))

    def chunks_v(q):
        return NR * q - chunks_a(q)

    RA, RV = 4, 8
    RI = 6

    slots = feature_slots(small, F)
    slot_of = {f: s for s, f in enumerate(slots)}
    TU = 4
    gathered = slots[1:F - len(small)]
    xunits = [gathered[i:i + TU] for i in range(0, len(gathered), TU)]
    NX = len(xunits)
    place = {f: k for k, f in enumerate(gathered)}

    GB = 4
    GU = 2 * GB
    NG = GROUPS // GU
    last = TILES - 1

    HB = B // 2
    TH = TILES // 2
    lookups = [(h, j) for h in range(2) for j in range(len(small))]
    FR = 3

    CH = 3
    rows, first_row = triangle(F, CH)
    KZ = sum(rows)
    PACKS = len(rows)
    WEIGHTS = 6


    def xposes(t, u0, u1):
        return [("xpose", t, u) for u in range(u0, min(u1, NX))]

    def grams(t):
        return [("gram", NG * t + v) for v in range(NG)]

    def woven(steps, others, start=0):
        out = []
        others = list(others)
        for n, x in enumerate(steps):
            out.append(x)
            if n >= start and others:
                out.append(others.pop(0))
        return out + others

    plan = woven([("small", q) for q in range(L)], xposes(0, 0, NX), 3)
    plan += woven(grams(0), xposes(1, 0, 2))
    plan += woven([("small", q) for q in range(L, L + L // 2)], xposes(1, 2, NX), 1)
    plan += grams(1) + [("layers", 0)]
    plan += woven([("small", q) for q in range(L + L // 2, 2 * L)], xposes(2, 0, NX))
    plan += grams(2) + [("layers", 1)] + xposes(3, 0, NX) + grams(3) + [("layers", 2), ("layers", 3)]

    xsteps = [x for x in plan if x[0] in ("small", "xpose")]

    def copier(x):
        return "dve" if x[0] == "xpose" and x[2] % 2 else "act"

    def copies_by(engine, x):
        return sum(copier(y) == engine for y in xsteps[:xsteps.index(x) + 1])

    def fills(x):
        return sum(y[0] != "small" for y in xsteps[:xsteps.index(x) + 1])

    ctx = ExitStack()
    with ctx:
        def sb(name, shape, dt=FP32):
            return ctx.enter_context(nc.sbuf_tensor(name, shape, dt))

        def pb(name, shape):
            return ctx.enter_context(nc.psum_tensor(name, shape, FP32))

        def sem(name):
            return ctx.enter_context(nc.semaphore(name))

        idx = sb("idx", [P, TILES, TABLES], INT32)
        ident = sb("ident", [P, P])
        row_int = sb("row_int", [P, NR], INT32)
        row = sb("row", [P, NR])
        minus_row = sb("minus_row", [P, NR])
        feat = sb("feat", [P, 2, len(gathered), D])
        whole = sb("whole", [Q, 2, NR, D])
        hi = sb("hi", [Q, L, NR, D], FP32R)
        lo = sb("lo", [Q, L, NR, D], FP32R)
        ids_all = sb("ids_all", [Q, RI, HB], INT32)
        distance = sb("distance", [Q, HB])
        onehot_a = sb("onehot_a", [Q, RA, HB], FP32R)
        onehot_v = sb("onehot_v", [Q, RV, HB], FP32R)
        featT = sb("featT", [D, FR * P, FS])
        bottomT = sb("bottomT", [D, B])
        z = sb("z", [F, F, P])
        zT = sb("zT", [P, 2, CH, P])
        w1z = sb("w1z", [KZ, CH, H1])
        w1b = sb("w1b", [D, H1])
        w2 = sb("w2", [P, N1, H2])
        w3 = sb("w3", [P, N2])
        b1c = sb("b1c", [P, N1])
        b2c = sb("b2c", [P, N2])
        h1 = sb("h1", [P, N1, P])
        h2 = sb("h2", [P, N2, P])
        y = sb("y", [1, B])

        psX = [pb(f"psX{i}", [P, TU, P]) for i in range(2)]
        psG = [pb(f"psG{i}", [P, 2, 512]) for i in range(2)]
        psL = [pb(f"psL{i}", [P, 4, P]) for i in range(2)]

        idx_in = sem("idx_in")
        bottom_in = sem("bottom_in")
        rows_in = [[sem(f"rows_in_{t}_{u}") for u in range(NX)] for t in range(TILES)]
        whole_in = [sem(f"whole_in_{i}") for i in range(2)]
        ids_in = [sem(f"ids_in_{i}") for i in range(RI)]
        weights_in = sem("weights_in")
        ident_zeroed = sem("ident_zeroed")
        ident_made = sem("ident_made")
        row_numbered = sem("row_numbered")
        row_made = sem("row_made")
        pads_zeroed = sem("pads_zeroed")
        hi_made = sem("hi_made")
        lo_made = sem("lo_made")
        distance_made = sem("distance_made")
        onehot_a_made = sem("onehot_a_made")
        onehot_v_made = sem("onehot_v_made")
        onehot_a_used = sem("onehot_a_used")
        onehot_v_used = sem("onehot_v_used")
        xfilled = sem("xfilled")
        xcopied_a = sem("xcopied_a")
        xcopied_v = sem("xcopied_v")
        gram_done = sem("gram_done")
        zcopied_a = sem("zcopied_a")
        zcopied_v = sem("zcopied_v")
        packed = [sem(f"packed_{i}") for i in range(2)]
        packed_by_pool = sem("packed_by_pool")
        l1_done = sem("l1_done")
        h1_a = sem("h1_a")
        h1_v = sem("h1_v")
        l2_done = sem("l2_done")
        h2_a = sem("h2_a")
        h2_v = sem("h2_v")
        l3_done = sem("l3_done")
        y_made = sem("y_made")
        y_out_done = sem("y_out_done")

        xcopied = {"act": xcopied_a, "dve": xcopied_v}

        block = ctx.enter_context(nc.Block())

        def gram_block(n, s):
            v = psG[n % 2][FS * s:FS * s + F, :, 0:GB * GS * F]
            return v.rearrange("i k (g s j) -> i s j k g", g=GB, s=GS)[:, s]

        def z_block(n, s):
            b0 = GS * GU * (n % NG)
            v = z[:, :, b0:b0 + GS * GU].rearrange("i j (k g s) -> i s j k g", k=2, s=GS)
            return v[:, s]

        def tileT(t):
            return featT[:, P * (t % FR):P * (t % FR + 1), :]

        def pack(eng, t, m, done):
            eng.dma_start(zT[first_row[m]:first_row[m] + rows[m], t % 2, :, :],
                          z[CH * m + 1:F, CH * m:CH * m + CH, :]).then_inc(done, 16)

        POOL_PACKS = 3

        @block.sync
        def _(sp):
            def load_ids(q):
                h, j = lookups[q]
                if q >= RI:
                    sp.wait_ge(onehot_a_made, chunks_a(q - RI + 1))
                    sp.wait_ge(onehot_v_made, chunks_v(q - RI + 1))
                sp.dma_start(ids_all[:, q % RI], ids_t[small[j] - 1:small[j], HB * h:HB * (h + 1)].to_broadcast([Q, HB])
                             ).then_inc(ids_in[q % RI], 16)

            def load_small(j):
                if j >= 2:
                    sp.wait_ge(lo_made, j - 1)
                sp.dma_start(whole[:, j % 2], tables[small[j] - 1].rearrange("(q r) d -> q r d", r=NR)
                             ).then_inc(whole_in[j % 2], 16)

            sp.dma_start(idx[:], ids.rearrange("(t p) f -> p t f", p=P)).then_inc(idx_in, 16)
            for j in range(2):
                load_small(j)
                load_ids(j)
            sp.dma_start(bottomT[:], bottom_t).then_inc(bottom_in, 16)
            for q in range(2, RI):
                load_ids(q)
            load_small(2)
            load_small(3)
            sp.dma_start(w1z[:], w1_pairs.rearrange("(c p) n -> p c n", c=CH)).then_inc(weights_in, 16)
            load_small(4)
            sp.dma_start(w1b[:], w1_bottom).then_inc(weights_in, 16)
            sp.dma_start(w2[:], W2.rearrange("(k p) n -> p k n", p=P)).then_inc(weights_in, 16)
            load_small(5)
            with nc.allow_non_contiguous_dma(reason="a bias or a weight column over partitions"):
                sp.dma_start(w3[:], W3.rearrange("(k p) o -> p (k o)", p=P)).then_inc(weights_in, 16)
                sp.dma_start(b1c[:], b1.rearrange("(k p) -> p k", p=P)).then_inc(weights_in, 16)
                sp.dma_start(b2c[:], b2.rearrange("(k p) -> p k", p=P)).then_inc(weights_in, 16)
            for j in range(6, L):
                load_ids(j)
                load_small(j)

            def pack_tile(t):
                sp.wait_ge(zcopied_a, 2 * NG * (t + 1))
                sp.wait_ge(zcopied_v, 2 * NG * (t + 1))
                if t >= 2:
                    sp.wait_ge(l1_done, N1 * (t - 1))
                for m in range(POOL_PACKS if t == last else 0, PACKS):
                    pack(sp, t, m, packed[t % 2])

            for kind, *at in plan:
                if kind == "small" and max(L, RI) <= at[0] + RI < 2 * L:
                    load_ids(at[0] + RI)
                elif kind == "gram" and at[0] % NG == NG - 1:
                    pack_tile(at[0] // NG)
            sp.wait_ge(y_made, TILES)
            sp.dma_start(y_out.rearrange("b o -> o b"), y[0:1, :]).then_inc(y_out_done, 16)
            sp.wait_ge(y_out_done, 16)

        @block.gpsimd
        def _(pool):
            nc.gpsimd.memset(ident[:], 0.0).then_inc(ident_zeroed, 1)
            nc.gpsimd.iota(row_int[:], pattern=[[1, NR]], base=0, channel_multiplier=NR).then_inc(row_numbered, 1)
            pool.wait_ge(ident_zeroed, 1)
            nc.gpsimd.affine_select(out=ident[:], in_=ident[:], compare_op=ALU.not_equal, fill=1.0, base=0,
                                    pattern=[[-1, P]], channel_multiplier=1).then_inc(ident_made, 1)
            pool.wait_ge(idx_in, 16)
            for t in range(TILES):
                for u, unit in enumerate(xunits):
                    if t >= 2:
                        pool.wait_ge(xfilled, fills(("xpose", t - 2, u)))
                    for f in unit:
                        nc.gpsimd.indirect_dma_start(
                            feat[:, t % 2, place[f], :], None, tables[f - 1],
                            bass.IndirectOffsetOnAxis(idx[:, t, f - 1:f], 0)).then_inc(rows_in[t][u], 16)
            pool.wait_ge(zcopied_a, 2 * NG * TILES)
            pool.wait_ge(zcopied_v, 2 * NG * TILES)
            pool.wait_ge(l1_done, N1 * (last - 1))
            for m in range(POOL_PACKS):
                pack(pool, last, m, packed_by_pool)

        @block.tensor
        def _(pe):
            def x_free(n):
                if n >= 2:
                    before = xsteps[n - 2]
                    pe.wait_ge(xcopied[copier(before)], copies_by(copier(before), before))

            def look_up(n, q):
                x_free(n)
                h, j = lookups[q]
                pe.wait_ge(hi_made, j + 1)
                pe.wait_ge(lo_made, j + 1)
                out = psX[n % 2][:, 0:TH, :].rearrange("d t b -> d (t b)")
                ca = by_act(q)
                for r in range(ca):
                    k = chunks_a(q) + r
                    pe.wait_ge(onehot_a_made, k + 1)
                    nc.tensor.matmul(out, hi[:, j, r, :], onehot_a[:, k % RA, :], start=(r == 0), stop=False)
                    nc.tensor.matmul(out, lo[:, j, r, :], onehot_a[:, k % RA, :], start=False, stop=False
                                     ).then_inc(onehot_a_used, 1)
                for r in range(ca, NR):
                    k = chunks_v(q) + r - ca
                    pe.wait_ge(onehot_v_made, k + 1)
                    nc.tensor.matmul(out, hi[:, j, r, :], onehot_v[:, k % RV, :], start=False, stop=False)
                    nc.tensor.matmul(out, lo[:, j, r, :], onehot_v[:, k % RV, :], start=False,
                                     stop=(r == NR - 1)).then_inc(onehot_v_used, 1)

            def transpose(n, t, u):
                x_free(n)
                pe.wait_ge(rows_in[t][u], 16 * len(xunits[u]))
                for k, f in enumerate(xunits[u]):
                    done = nc.tensor.transpose(psX[n % 2][:, k, :], feat[:, t % 2, place[f], :], ident[:])
                done.then_inc(xfilled, 1)

            def gram(n):
                t, v = n // NG, n % NG
                if v == 0:
                    pe.wait_ge(xcopied_a, max(copies_by("act", ("xpose", t, NX - 1)),
                                              copies_by("act", ("small", L * (t // TH + 1) - 1))))
                    pe.wait_ge(xcopied_v, copies_by("dve", ("xpose", t, NX - 1)))
                if n == 0:
                    pe.wait_ge(pads_zeroed, 1)
                if n >= 2:
                    pe.wait_ge(zcopied_a, 2 * (n - 1))
                    pe.wait_ge(zcopied_v, 2 * (n - 1))
                for g in range(GU):
                    b = GS * (GU * v + g)
                    four = tileT(t)[:, b:b + GS, :]
                    done = nc.tensor.matmul(psG[n % 2][:, g // GB, (g % GB) * GS * F:(g % GB + 1) * GS * F],
                                            four.rearrange("d s f -> d (s f)"), four[:, :, 0:F],
                                            start=True, stop=True)
                done.then_inc(gram_done, 1)

            def layers(t):
                if t == 0:
                    pe.wait_ge(weights_in, 16 * WEIGHTS)
                if t >= 1:
                    pe.wait_ge(h2_v, t)
                    pe.wait_ge(y_made, t)
                mine = POOL_PACKS if t == last else 0
                pe.wait_ge(packed[t % 2], 16 * (PACKS * (t // 2 + 1) - mine))
                if mine:
                    pe.wait_ge(packed_by_pool, 16 * mine)
                h1_read = (h1_a, h1_v)
                for o in range(N1):
                    if o >= 2:
                        pe.wait_ge(h1_read[o % 2], 2 * t + o // 2)
                    out = psL[o % 2][:, o // 2, :]
                    for c in range(CH):
                        nc.tensor.matmul(out, w1z[:, c, P * o:P * (o + 1)], zT[0:KZ, t % 2, c, :],
                                         start=(c == 0), stop=False)
                    nc.tensor.matmul(out, w1b[:, P * o:P * (o + 1)], bottomT[:, P * t:P * (t + 1)],
                                     start=False, stop=True).then_inc(l1_done, 1)
                pe.wait_ge(h1_a, 2 * (t + 1))
                for o in range(N2):
                    for c in range(N1):
                        if (o, c) == (0, N1 - 1):
                            pe.wait_ge(h1_v, 2 * (t + 1))
                        elif (o, c) == (0, 1):
                            pe.wait_ge(h1_v, 2 * t + 1)
                        done = nc.tensor.matmul(psL[o][:, 2, :], w2[:, c, P * o:P * (o + 1)],
                                                h1[:, c, :], start=(c == 0), stop=(c == N1 - 1))
                    done.then_inc(l2_done, 1)
                for c, ready in enumerate((h2_a, h2_v)):
                    pe.wait_ge(ready, t + 1)
                    done = nc.tensor.matmul(psL[0][0:1, 3, :], w3[:, c:c + 1], h2[:, c, :],
                                            start=(c == 0), stop=(c == N2 - 1))
                done.then_inc(l3_done, 1)

            pe.wait_ge(ident_made, 1)
            for kind, *at in plan:
                if kind == "small":
                    look_up(xsteps.index((kind, *at)), *at)
                elif kind == "xpose":
                    transpose(xsteps.index((kind, *at)), *at)
                elif kind == "layers":
                    layers(*at)
                else:
                    gram(*at)

        def copy_rows(eng_copy, t, u):
            k, s0 = len(xunits[u]), slot_of[xunits[u][0]]
            n = xsteps.index(("xpose", t, u))
            return eng_copy(tileT(t)[:, :, s0:s0 + k],
                            psX[n % 2][:, 0:k, :].rearrange("d f b -> d b f"))

        @block.scalar
        def _(act):
            def split_high(j):
                act.wait_ge(whole_in[j % 2], 16 * (j // 2 + 1))
                nc.scalar.activation(hi[:, j], whole[:, j % 2], ACT.Copy).then_inc(hi_made, 1)

            def make_onehot(q):
                act.wait_ge(ids_in[q % RI], 16 * (q // RI + 1))
                for r in range(by_act(q)):
                    k = chunks_a(q) + r
                    if k:
                        act.wait_ge(onehot_a_made, k)
                    nc.scalar.activation(distance[:], ids_all[:, q % RI], ACT.Abs,
                                         bias=minus_row[0:Q, r:r + 1]).then_inc(distance_made, 1)
                    act.wait_ge(distance_made, k + 1)
                    if k >= RA:
                        act.wait_ge(onehot_a_used, k - RA + 1)
                    nc.scalar.activation(onehot_a[:, k % RA, :], distance[:], ACT.Relu, bias=1.0,
                                         scale=-1.0).then_inc(onehot_a_made, 1)

            def copy_looked_up(q):
                h, j = lookups[q]
                n = xsteps.index(("small", q))
                act.wait_ge(onehot_v_used, chunks_v(q + 1))
                for t in range(TH * h, TH * (h + 1)):
                    if t >= FR and j == 0:
                        act.wait_ge(gram_done, NG * (t - FR + 1))
                    copied = nc.scalar.activation(tileT(t)[:, :, slot_of[small[j]]], psX[n % 2][:, t % TH, :], ACT.Copy)
                copied.then_inc(xcopied_a, 1)

            def copy_transposed(t, u):
                n = xsteps.index(("xpose", t, u))
                act.wait_ge(xfilled, fills(("xpose", t, u)))
                if u == 0:
                    act.wait_ge(bottom_in, 16)
                    nc.scalar.activation(tileT(t)[:, :, slot_of[0]], bottomT[:, P * t:P * (t + 1)], ACT.Copy)
                copy_rows(lambda out, in_: nc.scalar.activation(out, in_, ACT.Copy), t, u).then_inc(xcopied_a, 1)

            def copy_gram(n):
                t = n // NG
                if t and n % NG == 0:
                    act.wait_ge(packed[(t - 1) % 2], 16 * PACKS * ((t + 1) // 2))
                act.wait_ge(gram_done, n + 1)
                for s in (0, 1):
                    nc.scalar.activation(z_block(n, s), gram_block(n, s), ACT.Copy).then_inc(zcopied_a, 1)

            def layers(t):
                if t == 0:
                    act.wait_ge(weights_in, 16 * WEIGHTS)
                for o in (0, 2):
                    act.wait_ge(l1_done, N1 * t + o + 1)
                    nc.scalar.activation(h1[:, o, :], psL[0][:, o // 2, :], ACT.Relu,
                                         bias=b1c[:, o:o + 1]).then_inc(h1_a, 1)
                act.wait_ge(l2_done, N2 * t + 1)
                nc.scalar.activation(h2[:, 0, :], psL[0][:, 2, :], ACT.Relu, bias=b2c[:, 0:1]).then_inc(h2_a, 1)
                act.wait_ge(l3_done, t + 1)
                nc.scalar.activation(y[0:1, P * t:P * (t + 1)], psL[0][0:1, 3, :], ACT.Copy).then_inc(y_made, 1)

            split_high(0)
            act.wait_ge(row_made, 2)
            make_onehot(0)
            for kind, *at in plan:
                if kind == "small":
                    q, = at
                    if q + 1 < L:
                        split_high(q + 1)
                    if q + 1 < 2 * L:
                        make_onehot(q + 1)
                    copy_looked_up(q)
                elif kind == "xpose":
                    if copier((kind, *at)) == "act":
                        copy_transposed(*at)
                elif kind == "layers":
                    layers(*at)
                else:
                    copy_gram(*at)

        @block.vector
        def _(dve):
            def split_low(j):
                dve.wait_ge(hi_made, j + 1)
                nc.vector.tensor_tensor(lo[:, j], whole[:, j % 2], hi[:, j], ALU.subtract).then_inc(lo_made, 1)

            def make_onehot(q, chunks):
                dve.wait_ge(ids_in[q % RI], 16 * (q // RI + 1))
                for r in chunks:
                    k = chunks_v(q) + r - by_act(q)
                    if k >= RV:
                        dve.wait_ge(onehot_v_used, k - RV + 1)
                    nc.vector.tensor_scalar(onehot_v[:, k % RV, :], ids_all[:, q % RI], row[0:Q, r:r + 1],
                                            None, ALU.is_equal).then_inc(onehot_v_made, 1)

            def prepare(q):
                half = (by_act(q) + NR) // 2
                make_onehot(q, range(by_act(q), half))
                if q < L:
                    split_low(q)
                make_onehot(q, range(half, NR))

            def copy_transposed(t, u):
                dve.wait_ge(xfilled, fills(("xpose", t, u)))
                copy_rows(nc.vector.tensor_copy, t, u).then_inc(xcopied_v, 1)

            def copy_gram(n):
                t = n // NG
                if t and n % NG == 0:
                    dve.wait_ge(packed[(t - 1) % 2], 16 * PACKS * ((t + 1) // 2))
                dve.wait_ge(gram_done, n + 1)
                for s in (2, 3):
                    nc.vector.tensor_copy(z_block(n, s), gram_block(n, s)).then_inc(zcopied_v, 1)

            def layers(t):
                if t == 0:
                    dve.wait_ge(weights_in, 16 * WEIGHTS)
                for o in (1, 3):
                    dve.wait_ge(l1_done, N1 * t + o + 1)
                    nc.vector.tensor_scalar(h1[:, o, :], psL[1][:, o // 2, :], b1c[:, o:o + 1], 0.0,
                                            ALU.add, ALU.max).then_inc(h1_v, 1)
                dve.wait_ge(l2_done, N2 * t + 2)
                nc.vector.tensor_scalar(h2[:, 1, :], psL[1][:, 2, :], b2c[:, 1:2], 0.0,
                                        ALU.add, ALU.max).then_inc(h2_v, 1)

            dve.wait_ge(row_numbered, 1)
            nc.vector.tensor_copy(row[:], row_int[:]).then_inc(row_made, 1)
            dve.wait_ge(row_made, 1)
            nc.vector.tensor_scalar(minus_row[:], row[:], -1.0, None, ALU.mult).then_inc(row_made, 1)
            nc.vector.memset(featT[:, :, F:FS], 0.0).then_inc(pads_zeroed, 1)
            prepare(0)
            for kind, *at in plan:
                if kind == "small":
                    if at[0] + 1 < 2 * L:
                        prepare(at[0] + 1)
                elif kind == "xpose":
                    if copier((kind, *at)) == "dve":
                        copy_transposed(*at)
                elif kind == "layers":
                    layers(*at)
                else:
                    copy_gram(*at)


def kernel(**inputs):
    import numpy as _np
    import concourse.bacc as _bacc
    from concourse import mybir as _mybir
    from concourse.bass_utils import run_bass_kernel_spmd as _run

    nc = _bacc.Bacc("TRN2", target_bir_lowering=False, num_devices=1)
    F = 1 + inputs["ids"].shape[1]
    table_names = [f"tbl_{i}" for i in range(F - 1)]
    small = [f for f in range(1, F) if inputs[table_names[f - 1]].shape[0] == 1000]
    W1 = _np.asarray(inputs["W_top1"])
    slots, CH = feature_slots(small, F), 3
    rows, first_row = triangle(F, CH)
    w1_pairs = _np.zeros((CH, sum(rows), W1.shape[1]), W1.dtype)
    for i in range(F):
        for j in range(i + 1, F):
            f, g = sorted((slots[i], slots[j]))
            pair = f * (F - 1) - f * (f - 1) // 2 + g - f - 1
            w1_pairs[i % CH, first_row[i // CH] + j - (CH * (i // CH) + 1)] = W1[pair]
    laid_out = {
        "bottom_t": _np.asarray(inputs["r_bottom_output"]).T,
        "ids": inputs["ids"],
        "ids_t": _np.asarray(inputs["ids"]).T,
        "w1_pairs": w1_pairs.reshape(-1, W1.shape[1]),
        "w1_bottom": W1[F * (F - 1) // 2:],
        "b1": inputs["b_top1"], "W2": inputs["W_top2"], "b2": inputs["b_top2"], "W3": inputs["W_top3"],
        **{name: inputs[name] for name in table_names},
    }
    arrays, args = {}, {}
    for name, value in laid_out.items():
        a = _np.ascontiguousarray(value)
        arrays[f"in_{name}"] = a
        args[name] = nc.dram_tensor(f"in_{name}", a.shape, _mybir.dt.from_np(a.dtype), kind="ExternalInput").ap()
    y = nc.dram_tensor("out_y", (inputs["ids"].shape[0], 1), _mybir.dt.float32, kind="ExternalOutput").ap()
    dlrm_program(nc, args["bottom_t"], args["ids"], args["ids_t"], [args[n] for n in table_names], small,
                 args["w1_pairs"], args["w1_bottom"], args["b1"], args["W2"], args["b2"], args["W3"], y)
    r = _run(nc, [arrays], core_ids=[0])
    return r.results[0]["out_y"]
```

```python
from contextlib import ExitStack

import concourse.bass as bass
from concourse import mybir

FP32 = mybir.dt.float32
FP32R = mybir.dt.float32r
INT32 = mybir.dt.int32
ALU = mybir.AluOpType
ACT = mybir.ActivationFunctionType


def feature_slots(small, first_half, F):
    always = [f for f in range(1, F) if f not in small]
    return [0] + always + small[first_half:] + small[:first_half]


def triangle(F, CH):
    rows = [F - 1 - CH * m for m in range(F // CH)]
    return rows, [sum(rows[:m]) for m in range(len(rows))]


def dlrm_program(nc, bottom_t, ids, ids_t, tables, small, first_half, w1_pairs, w1_bottom, b1, W2, b2, W3, y_out):
    P = 128
    D, B = bottom_t.shape
    TABLES = len(tables)
    F = TABLES + 1
    TILES = B // P
    FS = 32
    GS = P // FS
    GROUPS = P // GS
    H1, H2 = W2.shape
    N1, N2 = H1 // P, H2 // P

    NR = 8
    Q = tables[small[0] - 1].shape[0] // NR
    assert all(tables[f - 1].shape[0] == NR * Q for f in small)
    PLAIN = 1
    HB = B // 2
    TH = TILES // 2
    lookups = [(0, j) for j in range(first_half)]
    lookups += [(1, j) for j in (*range(PLAIN, len(small)), *range(PLAIN))]
    LK = len(lookups)
    half_done = [first_half - 1, LK - 1]

    def splits(q):
        return q >= PLAIN and lookups[q][1] not in [j for _, j in lookups[PLAIN:q]]

    def splits_by(q):
        return sum(splits(i) for i in range(q + 1))

    loads = [q for q in range(LK) if q < PLAIN or splits(q)]
    WB = 5

    def load_parts(l):
        return [slice(0, Q)] if l < 2 else [slice(0, Q - Q % 16), slice(Q - Q % 16, Q)]

    def arrived(l):
        return 16 * sum(len(load_parts(i)) for i in range(l % WB, l + 1, WB))

    def split_no(j):
        return next(splits_by(q) for q in range(PLAIN, LK) if lookups[q][1] == j)

    PB = first_half - PLAIN

    def parts(j):
        return (split_no(j) - 1) % PB

    def by_act(q):
        return 1 + q % 2 if splits(q) else 2

    def chunks_a(q):
        return sum(by_act(i) for i in range(q))

    def chunks_v(q):
        return NR * q - chunks_a(q)

    RA, RV = 6, 20
    RI = 5

    slots = feature_slots(small, first_half, F)
    slot_of = {f: s for s, f in enumerate(slots)}
    TU = 4

    def gathered(t):
        return slots[1:F - (first_half if t < TH else len(small))]

    def xunits(t):
        g = gathered(t)
        return [g[i:i + TU] for i in range(0, len(g), TU)]

    place = {f: k for k, f in enumerate(gathered(0))}

    GB = 4
    GU = 2 * GB
    NG = GROUPS // GU
    last = TILES - 1

    FR = 3

    CH = 3
    rows, first_row = triangle(F, CH)
    KZ = sum(rows)
    PACKS = len(rows)
    WEIGHTS = 6

    STEPS = {"h": "high part", "l": "low part", "p": "one-hot", "s": "small", "x": "xpose",
             "g": "gram", "a": "layer 1", "b": "layer 2", "c": "layer 3"}

    def named(text):
        return [(STEPS[w[0]], int(w[1]), int(w[2])) if w[0] == "x" else (STEPS[w[0]], int(w[1:]))
                for w in text.split()]

    plan = named("""
        p0 p1 h1 l1 h2 p2 l2 h3 s0 p3 l3 h4 s1 p4 l4 s2 x00 p5 s3 x01 h5 l5 p6 s4 x02 h6 l6 s5 x03 x04 s6
        g0 p7 g1 x10 p8 g2 g3 x11
        s7 p9 s8 p10 s9 x12 p11 s10 x13 a0 p12 s11 x14 b0
        g4 x20 c0 h13 p13 l13 s12 g5 h14 p14 l14 g6 x21 g7
        s13 x22 s14 x23 x24 x30
        g8 g9 g10 g11 a1 x31 x32 b1 x33 x34 c1
        g12 g13 g14 g15 a2 b2 c2 a3 b3 c3""")

    needed = [("small", q) for q in range(LK)] + [("one-hot", q) for q in range(LK)]
    needed += [(part, q) for q in range(LK) if splits(q) for part in ("high part", "low part")]
    needed += [("xpose", t, u) for t in range(TILES) for u in range(len(xunits(t)))]
    needed += [("gram", n) for n in range(NG * TILES)]
    needed += [(f"layer {i}", t) for i in (1, 2, 3) for t in range(TILES)]
    assert sorted(plan) == sorted(needed)

    xsteps = [x for x in plan if x[0] in ("small", "xpose")]

    def copier(x):
        return "dve" if x[0] == "xpose" and x[1] and x[2] % 2 else "act"

    def copies_by(engine, x):
        return sum(copier(y) == engine for y in xsteps[:xsteps.index(x) + 1])

    def fills(x):
        return sum(y[0] != "small" for y in xsteps[:xsteps.index(x) + 1])

    ctx = ExitStack()
    with ctx:
        def sb(name, shape, dt=FP32):
            return ctx.enter_context(nc.sbuf_tensor(name, shape, dt))

        def pb(name, shape):
            return ctx.enter_context(nc.psum_tensor(name, shape, FP32))

        def sem(name):
            return ctx.enter_context(nc.semaphore(name))

        idx = sb("idx", [P, TILES, TABLES], INT32)
        ident = sb("ident", [P, P])
        row_int = sb("row_int", [P, NR], INT32)
        row = sb("row", [P, NR])
        minus_row = sb("minus_row", [P, NR])
        feat = sb("feat", [P, 2, len(gathered(0)), D])
        whole = sb("whole", [Q, WB, NR, D])
        hi = sb("hi", [Q, PB, NR, D], FP32R)
        lo = sb("lo", [Q, PB, NR, D], FP32R)
        ids_all = sb("ids_all", [Q, RI, HB], INT32)
        distance = sb("distance", [Q, HB])
        onehot_a = sb("onehot_a", [Q, RA, HB], FP32R)
        onehot_v = sb("onehot_v", [Q, RV, HB], FP32R)
        featT = sb("featT", [D, FR * P, FS])
        bottomT = sb("bottomT", [D, B])
        z = sb("z", [F, F, P])
        zT = sb("zT", [P, 2, CH, P])
        w1z = sb("w1z", [KZ, CH, H1])
        w1b = sb("w1b", [D, H1])
        w2 = sb("w2", [P, N1, H2])
        w3 = sb("w3", [P, N2])
        b1c = sb("b1c", [P, N1])
        b2c = sb("b2c", [P, N2])
        h1 = sb("h1", [P, N1, P])
        h2 = sb("h2", [P, N2, P])
        y = sb("y", [1, B])

        psX = [pb(f"psX{i}", [P, TU, P]) for i in range(2)]
        psG = [pb(f"psG{i}", [P, 2, 512]) for i in range(2)]
        psL = [pb(f"psL{i}", [P, 4, P]) for i in range(2)]

        idx_in = sem("idx_in")
        bottom_in = sem("bottom_in")
        rows_in = [[sem(f"rows_in_{t}_{u}") for u in range(len(xunits(t)))] for t in range(TILES)]
        whole_in = [sem(f"whole_in_{i}") for i in range(WB)]
        ids_in = [sem(f"ids_in_{i}") for i in range(RI)]
        weights_in = sem("weights_in")
        ident_zeroed = sem("ident_zeroed")
        ident_made = sem("ident_made")
        row_numbered = sem("row_numbered")
        row_made = sem("row_made")
        minus_row_made = sem("minus_row_made")
        pads_zeroed = sem("pads_zeroed")
        hi_made = sem("hi_made")
        lo_made = sem("lo_made")
        distance_made = sem("distance_made")
        onehot_a_made = sem("onehot_a_made")
        onehot_v_made = sem("onehot_v_made")
        onehot_a_used = sem("onehot_a_used")
        onehot_v_used = sem("onehot_v_used")
        xfilled = sem("xfilled")
        xcopied_a = sem("xcopied_a")
        xcopied_v = sem("xcopied_v")
        gram_done = sem("gram_done")
        zcopied_a = sem("zcopied_a")
        zcopied_v = sem("zcopied_v")
        packed = [sem(f"packed_{i}") for i in range(2)]
        packed_by_pool = sem("packed_by_pool")
        l1_done = sem("l1_done")
        h1_a = sem("h1_a")
        h1_v = sem("h1_v")
        l2_done = sem("l2_done")
        h2_a = sem("h2_a")
        h2_v = sem("h2_v")
        l3_done = sem("l3_done")
        y_made = sem("y_made")
        y_out_done = sem("y_out_done")

        xcopied = {"act": xcopied_a, "dve": xcopied_v}

        block = ctx.enter_context(nc.Block())

        def gram_block(n, s):
            v = psG[n % 2][FS * s:FS * s + F, :, 0:GB * GS * F]
            return v.rearrange("i k (g s j) -> i s j k g", g=GB, s=GS)[:, s]

        def z_block(n, s):
            b0 = GS * GU * (n % NG)
            v = z[:, :, b0:b0 + GS * GU].rearrange("i j (k g s) -> i s j k g", k=2, s=GS)
            return v[:, s]

        def tileT(t):
            b0 = P * ((t + 1) % FR)
            return featT[:, b0:b0 + P, :]

        def pack(eng, t, m, done):
            eng.dma_start(zT[first_row[m]:first_row[m] + rows[m], t % 2, :, :],
                          z[CH * m + 1:F, CH * m:CH * m + CH, :]).then_inc(done, 16)

        POOL_PACKS = 3

        @block.sync
        def _(sp):
            def load_ids(q):
                h, j = lookups[q]
                if q >= RI:
                    sp.wait_ge(onehot_a_made, chunks_a(q - RI + 1))
                    sp.wait_ge(onehot_v_made, chunks_v(q - RI + 1))
                sp.dma_start(ids_all[:, q % RI], ids_t[small[j] - 1:small[j], HB * h:HB * (h + 1)].to_broadcast([Q, HB])
                             ).then_inc(ids_in[q % RI], 16)

            def load_small(q):
                l = loads.index(q)
                if l >= WB:
                    before = loads[l - WB]
                    if before < PLAIN:
                        sp.wait_ge(onehot_a_used, chunks_a(before + 1))
                        sp.wait_ge(onehot_v_used, chunks_v(before + 1))
                    else:
                        sp.wait_ge(lo_made, splits_by(before))
                table = tables[small[lookups[q][1]] - 1].rearrange("(q r) d -> q r d", r=NR)
                for part in load_parts(l):
                    sp.dma_start(whole[part, l % WB], table[part]).then_inc(whole_in[l % WB], 16)

            sp.dma_start(idx[:], ids.rearrange("(t p) f -> p t f", p=P)).then_inc(idx_in, 16)
            for q in range(WB):
                load_ids(q)
                load_small(q)
            sp.dma_start(bottomT[:], bottom_t).then_inc(bottom_in, 16)
            WEIGHT_LOADS = [
                (w1z[:], w1_pairs.rearrange("(c p) n -> p c n", c=CH)),
                (w1b[:], w1_bottom),
                (w2[:], W2.rearrange("(k p) n -> p k n", p=P)),
                (w3[:], W3.rearrange("(k p) o -> p (k o)", p=P)),
                (b1c[:], b1.rearrange("(k p) -> p k", p=P)),
                (b2c[:], b2.rearrange("(k p) -> p k", p=P)),
            ]

            LOAD_AHEAD = 3
            WEIGHTS_AFTER = first_half

            def pack_tile(t):
                sp.wait_ge(zcopied_a, 2 * NG * (t + 1))
                sp.wait_ge(zcopied_v, 2 * NG * (t + 1))
                if t >= 2:
                    sp.wait_ge(l1_done, N1 * (t - 1))
                for m in range(POOL_PACKS if t == last else 0, PACKS):
                    pack(sp, t, m, packed[t % 2])

            for kind, *at in plan:
                if kind == "one-hot":
                    q, = at
                    if q + RI < LK:
                        load_ids(q + RI)
                    if q + LOAD_AHEAD in loads[WB:]:
                        load_small(q + LOAD_AHEAD)
                    if q == WEIGHTS_AFTER:
                        with nc.allow_non_contiguous_dma(reason="a bias or a weight column over partitions"):
                            for dst, src in WEIGHT_LOADS:
                                sp.dma_start(dst, src).then_inc(weights_in, 16)
                elif kind == "gram" and at[0] % NG == NG - 1:
                    pack_tile(at[0] // NG)
            sp.wait_ge(y_made, TILES)
            sp.dma_start(y_out.rearrange("b o -> o b"), y[0:1, :]).then_inc(y_out_done, 16)
            sp.wait_ge(y_out_done, 16)

        @block.gpsimd
        def _(pool):
            nc.gpsimd.memset(ident[:], 0.0).then_inc(ident_zeroed, 1)
            nc.gpsimd.iota(row_int[:], pattern=[[1, NR]], base=0, channel_multiplier=NR).then_inc(row_numbered, 1)
            pool.wait_ge(ident_zeroed, 1)
            nc.gpsimd.affine_select(out=ident[:], in_=ident[:], compare_op=ALU.not_equal, fill=1.0, base=0,
                                    pattern=[[-1, P]], channel_multiplier=1).then_inc(ident_made, 1)
            pool.wait_ge(idx_in, 16)
            for t in range(TILES):
                for u, unit in enumerate(xunits(t)):
                    if t >= 2:
                        pool.wait_ge(xfilled, fills(("xpose", t - 2, u)))
                    for f in unit:
                        nc.gpsimd.indirect_dma_start(
                            feat[:, t % 2, place[f], :], None, tables[f - 1],
                            bass.IndirectOffsetOnAxis(idx[:, t, f - 1:f], 0)).then_inc(rows_in[t][u], 16)
            pool.wait_ge(zcopied_a, 2 * NG * TILES)
            pool.wait_ge(zcopied_v, 2 * NG * TILES)
            pool.wait_ge(l1_done, N1 * (last - 1))
            for m in range(POOL_PACKS):
                pack(pool, last, m, packed_by_pool)

        @block.tensor
        def _(pe):
            def x_free(n):
                if n >= 2:
                    before = xsteps[n - 2]
                    pe.wait_ge(xcopied[copier(before)], copies_by(copier(before), before))

            def look_up(n, q):
                x_free(n)
                h, j = lookups[q]
                out = psX[n % 2][:, 0:TH, :].rearrange("d t b -> d (t b)")
                if q < PLAIN:
                    pe.wait_ge(whole_in[q % WB], arrived(q))
                else:
                    pe.wait_ge(hi_made, split_no(j))
                    pe.wait_ge(lo_made, split_no(j))
                ca = by_act(q)
                for r in range(NR):
                    if r < ca:
                        k = chunks_a(q) + r
                        onehot, made, used = onehot_a[:, k % RA, :], onehot_a_made, onehot_a_used
                    else:
                        k = chunks_v(q) + r - ca
                        onehot, made, used = onehot_v[:, k % RV, :], onehot_v_made, onehot_v_used
                    pe.wait_ge(made, k + 1)
                    if q < PLAIN:
                        done = nc.tensor.matmul(out, whole[:, q % WB, r, :], onehot.bitcast(FP32),
                                                start=(r == 0), stop=(r == NR - 1))
                    else:
                        nc.tensor.matmul(out, hi[:, parts(j), r, :], onehot, start=(r == 0), stop=False)
                        done = nc.tensor.matmul(out, lo[:, parts(j), r, :], onehot, start=False, stop=(r == NR - 1))
                    done.then_inc(used, 1)

            def transpose(n, t, u):
                x_free(n)
                pe.wait_ge(rows_in[t][u], 16 * len(xunits(t)[u]))
                for k, f in enumerate(xunits(t)[u]):
                    done = nc.tensor.transpose(psX[n % 2][:, k, :], feat[:, t % 2, place[f], :], ident[:])
                done.then_inc(xfilled, 1)

            def gram(n):
                t, v = n // NG, n % NG
                if v == 0:
                    newest = ("xpose", t, len(xunits(t)) - 1)
                    pe.wait_ge(xcopied_a, max(copies_by("act", newest),
                                              copies_by("act", ("small", half_done[t // TH]))))
                    if copies_by("dve", newest):
                        pe.wait_ge(xcopied_v, copies_by("dve", newest))
                if n == 0:
                    pe.wait_ge(pads_zeroed, 1)
                if n >= 2:
                    pe.wait_ge(zcopied_a, 2 * (n - 1))
                    pe.wait_ge(zcopied_v, 2 * (n - 1))
                for g in range(GU):
                    b = GS * (GU * v + g)
                    four = tileT(t)[:, b:b + GS, :]
                    done = nc.tensor.matmul(psG[n % 2][:, g // GB, (g % GB) * GS * F:(g % GB + 1) * GS * F],
                                            four.rearrange("d s f -> d (s f)"), four[:, :, 0:F],
                                            start=True, stop=True)
                done.then_inc(gram_done, 1)

            def layer_1(t):
                if t == 0:
                    pe.wait_ge(weights_in, 16 * WEIGHTS)
                h1_read = (h1_a, h1_v)
                for o in range(N1):
                    bank = (o + t) % 2
                    if o == 1 and t >= 1:
                        pe.wait_ge(y_made, t)
                    if o >= 2:
                        pe.wait_ge(h1_read[bank], 2 * t + o // 2)
                    out = psL[bank][:, o // 2, :]
                    nc.tensor.matmul(out, w1b[:, P * o:P * (o + 1)], bottomT[:, P * t:P * (t + 1)],
                                     start=True, stop=False)
                    if o == 0:
                        mine = POOL_PACKS if t == last else 0
                        pe.wait_ge(packed[t % 2], 16 * (PACKS * (t // 2 + 1) - mine))
                        if mine:
                            pe.wait_ge(packed_by_pool, 16 * mine)
                    for c in range(CH):
                        done = nc.tensor.matmul(out, w1z[:, c, P * o:P * (o + 1)], zT[0:KZ, t % 2, c, :],
                                                start=False, stop=(c == CH - 1))
                    done.then_inc(l1_done, 1)

            def layer_2(t):
                first, second = (h1_a, h1_v) if t % 2 == 0 else (h1_v, h1_a)
                pe.wait_ge(first, 2 * (t + 1))
                for o in range(N2):
                    for c in range(N1):
                        if (o, c) == (0, 1):
                            pe.wait_ge(second, 2 * t + 1)
                        elif (o, c) == (0, N1 - 1):
                            pe.wait_ge(second, 2 * (t + 1))
                        done = nc.tensor.matmul(psL[(o + t) % 2][:, 2, :], w2[:, c, P * o:P * (o + 1)],
                                                h1[:, c, :], start=(c == 0), stop=(c == N1 - 1))
                    done.then_inc(l2_done, 1)

            def layer_3(t):
                h2_made = (h2_a, h2_v)
                for c in range(N2):
                    pe.wait_ge(h2_made[(c + t) % 2], t + 1)
                    done = nc.tensor.matmul(psL[t % 2][0:1, 3, :], w3[:, c:c + 1], h2[:, c, :],
                                            start=(c == 0), stop=(c == N2 - 1))
                done.then_inc(l3_done, 1)

            pe.wait_ge(ident_made, 1)
            for kind, *at in plan:
                if kind == "small":
                    look_up(xsteps.index((kind, *at)), *at)
                elif kind == "xpose":
                    transpose(xsteps.index((kind, *at)), *at)
                elif kind == "gram":
                    gram(*at)
                elif kind == "layer 1":
                    layer_1(*at)
                elif kind == "layer 2":
                    layer_2(*at)
                elif kind == "layer 3":
                    layer_3(*at)

        def copy_rows(eng_copy, t, u):
            k, s0 = len(xunits(t)[u]), slot_of[xunits(t)[u][0]]
            n = xsteps.index(("xpose", t, u))
            return eng_copy(tileT(t)[:, :, s0:s0 + k],
                            psX[n % 2][:, 0:k, :].rearrange("d f b -> d b f"))

        @block.scalar
        def _(act):
            def split_high(q):
                l, j = loads.index(q), lookups[q][1]
                act.wait_ge(whole_in[l % WB], arrived(l))
                if split_no(j) > PB:
                    former = lookups[[i for i in loads if splits(i)][split_no(j) - 1 - PB]][1]
                    act.wait_ge(onehot_v_used, chunks_v(max(i for i in range(LK) if lookups[i][1] == former) + 1))
                nc.scalar.activation(hi[:, parts(j)], whole[:, l % WB], ACT.Copy).then_inc(hi_made, 1)

            def make_onehot(q):
                act.wait_ge(ids_in[q % RI], 16 * (q // RI + 1))
                for r in range(by_act(q)):
                    k = chunks_a(q) + r
                    if k:
                        act.wait_ge(onehot_a_made, k)
                    nc.scalar.activation(distance[:], ids_all[:, q % RI], ACT.Abs,
                                         bias=minus_row[0:Q, r:r + 1]).then_inc(distance_made, 1)
                    act.wait_ge(distance_made, k + 1)
                    if k >= RA:
                        act.wait_ge(onehot_a_used, k - RA + 1)
                    nc.scalar.activation(onehot_a[:, k % RA, :], distance[:], ACT.Relu, bias=1.0,
                                         scale=-1.0).then_inc(onehot_a_made, 1)

            def copy_looked_up(q):
                h, j = lookups[q]
                n = xsteps.index(("small", q))
                act.wait_ge(onehot_v_used, chunks_v(q + 1))
                t = TH * h
                if q == first_half:
                    act.wait_ge(gram_done, NG * (t + TH - FR))
                b0 = P * ((t + 1) % FR)
                nc.scalar.activation(featT[:, b0:b0 + HB, slot_of[small[j]]],
                                     psX[n % 2][:, 0:TH, :].rearrange("d t b -> d (t b)"),
                                     ACT.Copy).then_inc(xcopied_a, 1)

            def copy_transposed(t, u):
                n = xsteps.index(("xpose", t, u))
                act.wait_ge(xfilled, fills(("xpose", t, u)))
                if u == 0:
                    act.wait_ge(bottom_in, 16)
                    nc.scalar.activation(tileT(t)[:, :, slot_of[0]], bottomT[:, P * t:P * (t + 1)], ACT.Copy)
                copy_rows(lambda out, in_: nc.scalar.activation(out, in_, ACT.Copy), t, u).then_inc(xcopied_a, 1)

            def copy_gram(n):
                t = n // NG
                if t and n % NG == 0:
                    act.wait_ge(packed[(t - 1) % 2], 16 * PACKS * ((t + 1) // 2))
                act.wait_ge(gram_done, n + 1)
                for s in (0, 1):
                    nc.scalar.activation(z_block(n, s), gram_block(n, s), ACT.Copy).then_inc(zcopied_a, 1)

            def layer_1(t):
                if t == 0:
                    act.wait_ge(weights_in, 16 * WEIGHTS)
                for o in range(t % 2, N1, 2):
                    act.wait_ge(l1_done, N1 * t + o + 1)
                    nc.scalar.activation(h1[:, o, :], psL[0][:, o // 2, :], ACT.Relu,
                                         bias=b1c[:, o:o + 1]).then_inc(h1_a, 1)

            def layer_2(t):
                o = t % 2
                act.wait_ge(l2_done, N2 * t + o + 1)
                nc.scalar.activation(h2[:, o, :], psL[0][:, 2, :], ACT.Relu, bias=b2c[:, o:o + 1]).then_inc(h2_a, 1)

            def layer_3(t):
                if t % 2 == 0:
                    act.wait_ge(l3_done, t + 1)
                    nc.scalar.activation(y[0:1, P * t:P * (t + 1)], psL[0][0:1, 3, :], ACT.Copy).then_inc(y_made, 1)

            act.wait_ge(row_numbered, 1)
            nc.scalar.activation(minus_row[:], row_int[:], ACT.Copy, scale=-1.0).then_inc(minus_row_made, 1)
            act.wait_ge(minus_row_made, 1)
            for kind, *at in plan:
                if kind == "high part":
                    split_high(*at)
                elif kind == "one-hot":
                    make_onehot(*at)
                elif kind == "small":
                    copy_looked_up(*at)
                elif kind == "xpose":
                    if copier((kind, *at)) == "act":
                        copy_transposed(*at)
                elif kind == "gram":
                    copy_gram(*at)
                elif kind == "layer 1":
                    layer_1(*at)
                elif kind == "layer 2":
                    layer_2(*at)
                elif kind == "layer 3":
                    layer_3(*at)

        @block.vector
        def _(dve):
            def split_low(q):
                j = lookups[q][1]
                dve.wait_ge(hi_made, splits_by(q))
                nc.vector.tensor_tensor(lo[:, parts(j)], whole[:, loads.index(q) % WB], hi[:, parts(j)], ALU.subtract
                                        ).then_inc(lo_made, 1)

            def make_onehot(q):
                dve.wait_ge(ids_in[q % RI], 16 * (q // RI + 1))
                for r in range(by_act(q), NR):
                    k = chunks_v(q) + r - by_act(q)
                    if k >= RV:
                        dve.wait_ge(onehot_v_used, k - RV + 1)
                    nc.vector.tensor_scalar(onehot_v[:, k % RV, :], ids_all[:, q % RI], row[0:Q, r:r + 1],
                                            None, ALU.is_equal).then_inc(onehot_v_made, 1)

            def copy_transposed(t, u):
                dve.wait_ge(xfilled, fills(("xpose", t, u)))
                copy_rows(nc.vector.tensor_copy, t, u).then_inc(xcopied_v, 1)

            def copy_gram(n):
                t = n // NG
                if t and n % NG == 0:
                    dve.wait_ge(packed[(t - 1) % 2], 16 * PACKS * ((t + 1) // 2))
                dve.wait_ge(gram_done, n + 1)
                for s in (2, 3):
                    nc.vector.tensor_copy(z_block(n, s), gram_block(n, s)).then_inc(zcopied_v, 1)

            def layer_1(t):
                if t == 0:
                    dve.wait_ge(weights_in, 16 * WEIGHTS)
                for o in range(1 - t % 2, N1, 2):
                    dve.wait_ge(l1_done, N1 * t + o + 1)
                    nc.vector.tensor_scalar(h1[:, o, :], psL[1][:, o // 2, :], b1c[:, o:o + 1], 0.0,
                                            ALU.add, ALU.max).then_inc(h1_v, 1)

            def layer_2(t):
                o = 1 - t % 2
                dve.wait_ge(l2_done, N2 * t + o + 1)
                nc.vector.tensor_scalar(h2[:, o, :], psL[1][:, 2, :], b2c[:, o:o + 1], 0.0,
                                        ALU.add, ALU.max).then_inc(h2_v, 1)

            def layer_3(t):
                if t % 2:
                    dve.wait_ge(l3_done, t + 1)
                    nc.vector.tensor_copy(y[0:1, P * t:P * (t + 1)], psL[1][0:1, 3, :]).then_inc(y_made, 1)

            dve.wait_ge(row_numbered, 1)
            nc.vector.tensor_copy(row[:], row_int[:]).then_inc(row_made, 1)
            dve.wait_ge(row_made, 1)
            nc.vector.memset(featT[:, :, F:FS], 0.0).then_inc(pads_zeroed, 1)
            for kind, *at in plan:
                if kind == "low part":
                    split_low(*at)
                elif kind == "one-hot":
                    make_onehot(*at)
                elif kind == "xpose":
                    if copier((kind, *at)) == "dve":
                        copy_transposed(*at)
                elif kind == "gram":
                    copy_gram(*at)
                elif kind == "layer 1":
                    layer_1(*at)
                elif kind == "layer 2":
                    layer_2(*at)
                elif kind == "layer 3":
                    layer_3(*at)


def kernel(**inputs):
    import numpy as _np
    import concourse.bacc as _bacc
    from concourse import mybir as _mybir
    from concourse.bass_utils import run_bass_kernel_spmd as _run

    nc = _bacc.Bacc("TRN2", target_bir_lowering=False, num_devices=1)
    F = 1 + inputs["ids"].shape[1]
    table_names = [f"tbl_{i}" for i in range(F - 1)]
    small = [f for f in range(1, F) if inputs[table_names[f - 1]].shape[0] == 1000][:8]
    first_half = 7
    W1 = _np.asarray(inputs["W_top1"])
    slots, CH = feature_slots(small, first_half, F), 3
    rows, first_row = triangle(F, CH)
    w1_pairs = _np.zeros((CH, sum(rows), W1.shape[1]), W1.dtype)
    for i in range(F):
        for j in range(i + 1, F):
            f, g = sorted((slots[i], slots[j]))
            pair = f * (F - 1) - f * (f - 1) // 2 + g - f - 1
            w1_pairs[i % CH, first_row[i // CH] + j - (CH * (i // CH) + 1)] = W1[pair]
    laid_out = {
        "bottom_t": _np.asarray(inputs["r_bottom_output"]).T,
        "ids": inputs["ids"],
        "ids_t": _np.asarray(inputs["ids"]).T,
        "w1_pairs": w1_pairs.reshape(-1, W1.shape[1]),
        "w1_bottom": W1[F * (F - 1) // 2:],
        "b1": inputs["b_top1"], "W2": inputs["W_top2"], "b2": inputs["b_top2"], "W3": inputs["W_top3"],
        **{name: inputs[name] for name in table_names},
    }
    arrays, args = {}, {}
    for name, value in laid_out.items():
        a = _np.ascontiguousarray(value)
        arrays[f"in_{name}"] = a
        args[name] = nc.dram_tensor(f"in_{name}", a.shape, _mybir.dt.from_np(a.dtype), kind="ExternalInput").ap()
    y = nc.dram_tensor("out_y", (inputs["ids"].shape[0], 1), _mybir.dt.float32, kind="ExternalOutput").ap()
    dlrm_program(nc, args["bottom_t"], args["ids"], args["ids_t"], [args[n] for n in table_names], small, first_half,
                 args["w1_pairs"], args["w1_bottom"], args["b1"], args["W2"], args["b2"], args["W3"], y)
    r = _run(nc, [arrays], core_ids=[0])
    return r.results[0]["out_y"]
```
